# Optimizing a Trainium2 kernel written in Bass

```python
import numpy as np
import jax
import jax.numpy as jnp

def _softmax(x, axis=-1):
    return jax.nn.softmax(x, axis=axis)

def _gelu(x):
    return jax.nn.gelu(x, approximate=True)

def _silu(x):
    return jax.nn.silu(x)

def _sigmoid(x):
    return jax.nn.sigmoid(x)

def _layernorm(x, axis=-1, eps=1e-05):
    m = jnp.mean(x, axis=axis, keepdims=True)
    v = jnp.var(x, axis=axis, keepdims=True)
    return (x - m) / jnp.sqrt(v + eps)

def _scatter_add(tgt, idx, src, axis=0):
    return tgt.at[idx].add(src)

def _segment_sum(src, seg, n):
    return jax.ops.segment_sum(src, seg, n)
kernel_name = 'mk_gnn_ffn_d2_gnn_r8_35c4f3'

def setup_inputs(seed: int=0):
    np.random.seed(seed)
    _w = jnp.asarray

    def _rec_inputs():
        import jax
        import jax.numpy as jnp
        _gk = jax.random.key(seed)
        x = -0.0003713 + 1 * jax.random.normal(jax.random.fold_in(_gk, 1), (6250, 256), jnp.float32)
        src = jax.random.randint(jax.random.fold_in(_gk, 2), (100000,), 0, 6250, jnp.int32)
        dst = jax.random.randint(jax.random.fold_in(_gk, 3), (100000,), 0, 6250, jnp.int32)
        _o = jnp.argsort(dst, stable=True)
        src = src[_o]
        dst = dst[_o]
        return (x, src, dst)
    x, src, dst = _rec_inputs()

    def _L0_gnn_setup():
        import jax, jax.numpy as jnp
        import numpy as np
        N = 6250
        E = 100000
        IN_C = 256
        HEADS = 8
        OUT_C = 32
        NEG_SLOPE = 0.2
        key = jax.random.key(seed)
        k1, k2, k3, k4, k5 = jax.random.split(key, 5)
        x = jax.random.normal(k1, (N, IN_C), dtype=jnp.float32)
        edge_index = jax.random.randint(k2, (2, E), 0, N, dtype=jnp.int64)
        W = jax.random.normal(k3, (IN_C, HEADS * OUT_C), dtype=jnp.float32) * (1.0 / np.sqrt(IN_C))
        attn_l = jax.random.normal(k4, (1, HEADS, OUT_C), dtype=jnp.float32) * 0.1
        attn_r = jax.random.normal(k5, (1, HEADS, OUT_C), dtype=jnp.float32) * 0.1
        bias = jnp.zeros((HEADS * OUT_C,), dtype=jnp.float32)
        return {'x': x, 'edge_index': edge_index, 'W': W, 'attn_l': attn_l, 'attn_r': attn_r, 'bias': bias}
    _L0_gnn_all = _L0_gnn_setup()
    _L0_gnn_in = {k: v for k, v in _L0_gnn_all.items() if k in ('W', 'attn_l', 'attn_r', 'bias')}
    del _L0_gnn_all

    def _L0_ffn_setup():
        import jax, jax.numpy as jnp
        import numpy as np
        E, D, H, TOP_K = (6, 256, 256, 2)
        ROUTER_H = D // 2
        key = jax.random.key(seed)
        ks = jax.random.split(key, 12)
        s = 1.0 / np.sqrt(D)
        sh = 1.0 / np.sqrt(H)
        sr = 1.0 / np.sqrt(ROUTER_H)
        return {'features': jax.random.normal(ks[0], (8, 512, D), dtype=jnp.float32), 'router_w1': jax.random.uniform(ks[1], (D, ROUTER_H), jnp.float32, -s, s), 'router_b1': jnp.zeros((ROUTER_H,), jnp.float32), 'router_w2': jax.random.uniform(ks[2], (ROUTER_H, E), jnp.float32, -sr, sr), 'router_b2': jnp.zeros((E,), jnp.float32), 'expert_w1': jax.random.uniform(ks[3], (E, D, H), jnp.float32, -s, s), 'expert_b1': jnp.zeros((E, H), jnp.float32), 'expert_w2': jax.random.uniform(ks[4], (E, H, H), jnp.float32, -sh, sh), 'expert_b2': jnp.zeros((E, H), jnp.float32), 'expert_w3': jax.random.uniform(ks[5], (E, H, D), jnp.float32, -sh, sh), 'expert_b3': jnp.zeros((E, D), jnp.float32)}
    _L0_ffn_all = _L0_ffn_setup()
    _L0_ffn_in = {k: v for k, v in _L0_ffn_all.items() if k in ('router_w1', 'router_b1', 'router_w2', 'router_b2', 'expert_w1', 'expert_b1', 'expert_w2', 'expert_b2', 'expert_w3', 'expert_b3')}
    del _L0_ffn_all

    def _L1_gnn_setup():
        import jax, jax.numpy as jnp
        import numpy as np
        N_NODES = 6250
        key = jax.random.key(seed)
        k1, k2, k3 = jax.random.split(key, 3)
        x = jax.random.normal(k1, (N_NODES, 256), dtype=jnp.float32)
        W = jax.random.normal(k2, (256, 256), dtype=jnp.float32) * (1.0 / np.sqrt(256))
        edge_index = jax.random.randint(k3, (2, 200000), 0, N_NODES, dtype=jnp.int64)
        return {'x': x, 'W': W, 'edge_index': edge_index}
    _L1_gnn_all = _L1_gnn_setup()
    _L1_gnn_in = {k: v for k, v in _L1_gnn_all.items() if k in ('W',)}
    del _L1_gnn_all

    def _L1_ffn_setup():
        import jax, jax.numpy as jnp
        import numpy as np
        B, S, D = (8, 512, 256)
        H = 4 * D
        CAPACITY = 0.5
        key = jax.random.key(seed)
        ks = jax.random.split(key, 6)
        x = jax.random.normal(ks[0], (B, S, D), dtype=jnp.float32)
        attention_mask = jnp.zeros((B, 1, 1, S), dtype=jnp.float32)
        wr = jax.random.normal(ks[1], (D, 1), dtype=jnp.float32) * 0.02
        br = jnp.zeros((1,), dtype=jnp.float32)
        w1 = jax.random.normal(ks[2], (D, H), dtype=jnp.float32) * 0.02
        b1 = jnp.zeros((H,), dtype=jnp.float32)
        w2 = jax.random.normal(ks[3], (H, D), dtype=jnp.float32) * 0.02
        b2 = jnp.zeros((D,), dtype=jnp.float32)
        return {'x': x, 'attention_mask': attention_mask, 'wr': wr, 'br': br, 'w1': w1, 'b1': b1, 'w2': w2, 'b2': b2}
    _L1_ffn_all = _L1_ffn_setup()
    _L1_ffn_in = {k: v for k, v in _L1_ffn_all.items() if k in ('attention_mask', 'wr', 'br', 'w1', 'b1', 'w2', 'b2')}
    del _L1_ffn_all
    return {'x': x, 'src': src, 'dst': dst, 'L0_gnn_W': _L0_gnn_in['W'], 'L0_gnn_attn_l': _L0_gnn_in['attn_l'], 'L0_gnn_attn_r': _L0_gnn_in['attn_r'], 'L0_gnn_bias': _L0_gnn_in['bias'], 'L0_ffn_router_w1': _L0_ffn_in['router_w1'], 'L0_ffn_router_b1': _L0_ffn_in['router_b1'], 'L0_ffn_router_w2': _L0_ffn_in['router_w2'], 'L0_ffn_router_b2': _L0_ffn_in['router_b2'], 'L0_ffn_expert_w1': _L0_ffn_in['expert_w1'], 'L0_ffn_expert_b1': _L0_ffn_in['expert_b1'], 'L0_ffn_expert_w2': _L0_ffn_in['expert_w2'], 'L0_ffn_expert_b2': _L0_ffn_in['expert_b2'], 'L0_ffn_expert_w3': _L0_ffn_in['expert_w3'], 'L0_ffn_expert_b3': _L0_ffn_in['expert_b3'], 'L1_gnn_W': _L1_gnn_in['W'], 'L1_ffn_attention_mask': _L1_ffn_in['attention_mask'], 'L1_ffn_wr': _L1_ffn_in['wr'], 'L1_ffn_br': _L1_ffn_in['br'], 'L1_ffn_w1': _L1_ffn_in['w1'], 'L1_ffn_b1': _L1_ffn_in['b1'], 'L1_ffn_w2': _L1_ffn_in['w2'], 'L1_ffn_b2': _L1_ffn_in['b2']}

def reference(x, src, dst, L0_gnn_W, L0_gnn_attn_l, L0_gnn_attn_r, L0_gnn_bias, L0_ffn_router_w1, L0_ffn_router_b1, L0_ffn_router_w2, L0_ffn_router_b2, L0_ffn_expert_w1, L0_ffn_expert_b1, L0_ffn_expert_w2, L0_ffn_expert_b2, L0_ffn_expert_w3, L0_ffn_expert_b3, L1_gnn_W, L1_ffn_attention_mask, L1_ffn_wr, L1_ffn_br, L1_ffn_w1, L1_ffn_b1, L1_ffn_w2, L1_ffn_b2):
    import jax
    import jax.numpy as jnp

    def _L0_gnn_ref(x, edge_index, W, attn_l, attn_r, bias):
        import jax, jax.numpy as jnp
        import numpy as np
        N = 6250
        E = 100000
        IN_C = 256
        HEADS = 8
        OUT_C = 32
        NEG_SLOPE = 0.2
        n = x.shape[0]
        h = (x @ W).reshape(n, HEADS, OUT_C)
        a1 = jnp.sum(h * attn_l, axis=-1)
        a2 = jnp.sum(h * attn_r, axis=-1)
        src, dst = (edge_index[0], edge_index[1])
        e = a1[src] + a2[dst]
        e = jax.nn.leaky_relu(e, negative_slope=NEG_SLOPE)
        seg_max = jax.ops.segment_max(e, dst, num_segments=n)
        seg_max = jnp.where(jnp.isfinite(seg_max), seg_max, 0.0)
        ex = jnp.exp(e - seg_max[dst])
        denom = jax.ops.segment_sum(ex, dst, num_segments=n)
        alpha = ex / denom[dst]
        message = h[src] * alpha[:, :, None]
        out = jax.ops.segment_sum(message, dst, num_segments=n)
        out = out.reshape(n, HEADS * OUT_C)
        return out + bias

    def _L0_ffn_ref(features, router_w1, router_b1, router_w2, router_b2, expert_w1, expert_b1, expert_w2, expert_b2, expert_w3, expert_b3):
        import jax, jax.numpy as jnp
        import numpy as np
        E, D, H, TOP_K = (6, 256, 256, 2)
        ROUTER_H = D // 2
        rh = jax.nn.relu(features @ router_w1 + router_b1)
        expert_logits = jax.nn.softmax(rh @ router_w2 + router_b2, axis=-1)
        top_w, top_i = jax.lax.top_k(expert_logits, TOP_K)
        routing_weights = jax.nn.softmax(top_w, axis=-1)
        h1 = jax.nn.relu(jnp.einsum('bsd,edh->bseh', features, expert_w1) + expert_b1)
        h2 = jax.nn.relu(jnp.einsum('bseh,ehf->bsef', h1, expert_w2) + expert_b2)
        expert_out = jnp.einsum('bsef,efo->bseo', h2, expert_w3) + expert_b3
        sel = jnp.take_along_axis(expert_out, top_i[:, :, :, None], axis=2)
        combined = jnp.sum(sel * routing_weights[..., None], axis=2)
        return combined

    def _L1_gnn_ref(x, W, edge_index):
        import jax, jax.numpy as jnp
        import numpy as np
        N_NODES = 6250
        N = x.shape[0]
        src, dst = (edge_index[0], edge_index[1])
        h = x @ W
        deg = jax.ops.segment_sum(jnp.ones_like(dst, dtype=h.dtype), dst, num_segments=N)
        deg_inv_sqrt = jnp.where(deg > 0, jax.lax.rsqrt(jnp.maximum(deg, 1)), 0.0)
        norm = deg_inv_sqrt[src] * deg_inv_sqrt[dst]
        msgs = h[src] * norm[:, None]
        out = jax.ops.segment_sum(msgs, dst, num_segments=N)
        return out

    def _L1_ffn_ref(x, attention_mask, wr, br, w1, b1, w2, b2):
        import jax, jax.numpy as jnp
        import numpy as np
        B, S, D = (8, 512, 256)
        H = 4 * D
        CAPACITY = 0.5
        b, s, d = x.shape
        weights = (jnp.einsum('bsd,do->bso', x, wr) + br)[..., 0]
        k = max(1, int(CAPACITY * s))
        kk = k - 1 if k > 1 else 1
        _, idx = jax.lax.top_k(weights, k)
        sel_idx = idx[:, :kk]
        sel = jnp.take_along_axis(x, sel_idx[:, :, None], axis=1)
        h = jax.nn.gelu(jnp.einsum('bkd,dh->bkh', sel, w1) + b1)
        y = jnp.einsum('bkh,hd->bkd', h, w2) + b2
        w_sel = jnp.take_along_axis(weights, sel_idx, axis=1)
        y = y * w_sel[..., None]
        batch_idx = jnp.arange(b)[:, None]
        processed = jnp.zeros_like(x).at[batch_idx, sel_idx].set(y)
        return processed + x
    edge_index = jnp.stack([src, dst])
    x = x + _L0_gnn_ref(_layernorm(x, axis=-1), edge_index, L0_gnn_W, L0_gnn_attn_l, L0_gnn_attn_r, L0_gnn_bias)
    x = x + _L0_ffn_ref(_layernorm(x, axis=-1)[None], L0_ffn_router_w1, L0_ffn_router_b1, L0_ffn_router_w2, L0_ffn_router_b2, L0_ffn_expert_w1, L0_ffn_expert_b1, L0_ffn_expert_w2, L0_ffn_expert_b2, L0_ffn_expert_w3, L0_ffn_expert_b3)[0]
    x = x + _L1_gnn_ref(_layernorm(x, axis=-1), L1_gnn_W, edge_index)
    x = x + _L1_ffn_ref(_layernorm(x, axis=-1)[None], L1_ffn_attention_mask, L1_ffn_wr, L1_ffn_br, L1_ffn_w1, L1_ffn_b1, L1_ffn_w2, L1_ffn_b2)[0]
    return x

_drawn_inputs = setup_inputs


def setup_inputs(seed=0):
    import zlib

    import numpy as np

    out = dict(_drawn_inputs(seed))
    spreads = {'L0_gnn_bias': (0.0, 0.1),
     'L0_ffn_router_b1': (0.0, 0.1),
     'L0_ffn_router_b2': (0.0, 0.1),
     'L0_ffn_expert_b1': (0.0, 0.682),
     'L0_ffn_expert_b2': (0.0, 0.272),
     'L0_ffn_expert_b3': (0.0, 0.1),
     'L1_ffn_b1': (0.0, 0.8),
     'L1_ffn_b2': (0.0, 0.665)}
    factors = {'L1_ffn_wr': 3.921, 'L1_ffn_w1': 4.619, 'L1_ffn_w2': 4.292}
    for name, (base, spread) in spreads.items():
        noise = np.random.default_rng([zlib.crc32(name.encode()), seed]).standard_normal(out[name].shape)
        drawn = base * np.exp(spread * noise) if base else spread * noise
        out[name] = jnp.asarray(drawn.astype(out[name].dtype))
    for name, factor in factors.items():
        out[name] = (out[name] * factor).astype(out[name].dtype)
    return out
```

```python
import concourse.bass as bass
from concourse import mybir
from contextlib import ExitStack

P = 128
N = 6250
D = 256
E = 100000
HEADS, C = 8, 32
NT = -(-N // P)
LASTROWS = N - (NT - 1) * P
ET = -(-E // P)
EROWS = 784
NOWHERE = 8191
KD = D // P
NX, RH_, HF = 6, 128, 1024
CAP = max(1, int(0.5 * N)) - 1

W = 4
NWIN = -(-(ET + NT - 1) // W)
RING = 11
FWIN = NWIN + 1
assert FWIN % RING == 0 and NWIN % 2 == 0
JT = 7
GT_ = 4
NG = (NT - 1) // GT_
AW = D + HEADS
MW = AW + 1
PAIR = KD * P


class Items:

    def __init__(self, order, group, full):
        self.order, self.group = order, group
        self.at = {name: n for n, (name, _) in enumerate(order)}
        full = full or order
        self.total = len(full)
        self.totals = {c: sum(1 for _, k in full if k == c) for c in ("act", "dve")}

    def taken(self, name):
        n = self.at[name]
        c = self.order[n][1]
        return c, self.group * self.totals[c] + sum(1 for _, k in self.order[: n + 1] if k == c)

    def made(self, name):
        return self.group * self.total + self.at[name] + 1


def moe_order(nt):
    half = [0, 1] if nt > 2 else [0]
    o = [("xt0", "act"), ("xt1", "dve"), ("rh", "act")]
    h1 = lambda e: [(f"h1_{e}_0", "act"), (f"h1_{e}_1", "dve")]
    h2 = lambda e: [(f"h2_{e}_0", "act"), (f"h2_{e}_1", "dve")]
    out = lambda e: [(f"o_{e}_{h}", "dve") for h in half]
    o += h1(0) + h1(1) + [("lg", "dve")] + h2(0)
    for e in range(1, NX):
        o += (h1(e + 1) if e + 1 < NX else [])
        o += out(e - 1)
        if e == 1:
            o += [("gt", "act")]
        o += h2(e)
    o += [(f"b3_{h}", "dve") for h in half] + out(NX - 1)
    o += [("xu0", "act"), ("xu1", "dve")] + [(f"p_{h}", "act") for h in half]
    return o


def ffn_order(nt):
    half = [0, 1] if nt > 2 else [0]
    o = [("xt0", "act"), ("xt1", "dve"), ("wt", "dve")]
    o += [(f"h_{m}", "act") for m in range(HF // P)]
    o += [(f"y_{h}", "dve") for h in half]
    return o


def gnn_kernel(nc, A, out, stage):
    f32, i32 = mybir.dt.float32, mybir.dt.int32
    ALU, ACT, AX = mybir.AluOpType, mybir.ActivationFunctionType, mybir.AxisListType
    ds = bass.ds
    ht0 = nc.dram_tensor("ht0", (NT * P, AW), f32, kind="Internal").ap()
    ht1 = nc.dram_tensor("ht1", (NT * P, D), f32, kind="Internal").ap()
    yd = nc.dram_tensor("yd", (NT * P, D), f32, kind="Internal").ap()

    ctx = ExitStack()
    with ctx:
        def sb(name, shape, dt=f32):
            return ctx.enter_context(nc.sbuf_tensor(name, shape, dt))

        def sem(name):
            return ctx.enter_context(nc.semaphore(name))

        X = sb("X", [P, NT, D])
        ring = sb("ring", [P, RING * W, AW])
        idxp = sb("idxp", [P, JT * P], i32)
        dloc = sb("dloc", [P, JT * P])
        tab = sb("tab", [1, FWIN, 6], mybir.dt.int16)
        idxs = sb("idxs", [P, RING, W], i32)
        S = sb("S", [P, 2, W, P])
        ST = sb("ST", [P, 2, W, P])
        M = sb("M", [P, 2, W, MW])
        acc = sb("acc", [P, 2 * GT_, MW])
        a2sh = sb("a2sh", [P, NT, 16])
        dinv = sb("dinv", [P, NT])
        iotaf = sb("iotaf", [P, P])
        ident = sb("ident", [P, P])
        ones = sb("ones", [P, P])
        zero = sb("zero", [P, 1])
        pidf = sb("pidf", [P, 1])
        rev = sb("rev", [P, NX])
        wext = sb("wext", [P, KD, D + 16])
        w1g = sb("w1g", [P, KD, D])
        bias0 = sb("bias0", [P, D])
        ew = [sb(f"ew{i}", [P, NX, KD, D]) for i in range(3)]
        eb = sb("eb", [P, 2, NX, KD])
        eb3 = sb("eb3", [NX, D])
        rw1 = sb("rw1", [P, KD, RH_])
        rb1 = sb("rb1", [P, 1])
        rw2 = sb("rw2", [P, NX])
        rb2 = sb("rb2", [P, NX])
        XN = sb("XN", [P, GT_, D])
        XT = sb("XT", [P, KD, GT_ * P])
        H1 = sb("H1", [P, 2, KD, GT_ * P])
        H2 = sb("H2", [P, KD, GT_ * P])
        rhT = sb("rhT", [P, GT_ * P])
        gate = sb("gate", [P, GT_, 8])
        rt = sb("rt", [P, 6, GT_, NX])
        rs = sb("rs", [P, 8, GT_])
        e1 = sb("e1", [P, W, HEADS])
        e2 = sb("e2", [P, W, HEADS])
        rden = sb("rden", [P, GT_, HEADS])
        st6 = sb("st6", [P, GT_, 6])
        mv = sb("mv", [P, 6, GT_])
        sq = sb("sq", [P, 2 * GT_])
        sqr = sb("sqr", [P, 2 * GT_])
        rc = sb("rc", [P, 2 * GT_])
        ind = sb("ind", [P, GT_])
        last = sb("last", [112, 7], i32)
        lastf = sb("lastf", [112, 7])
        attn = sb("attn", [P, 4])
        mx = sb("mx", [P, 4 * HEADS])
        ti32 = H1[:, :, :, :].rearrange("p a b c -> p (a b c)").bitcast(i32)
        jrow_i, iota_i = ti32[:, 0:JT * P], ti32[:, JT * P:JT * P + P]
        t128_i, jcol_i, pid_i = ti32[:, 1024:1072], ti32[:, 1072:1079], ti32[:, 1079:1080]
        hm_i = ti32[:, 1080:1096]
        kcol = ti32[:, 1100:1107]
        H2f = H2[:, :, :].rearrange("p a b -> p (a b)")
        jrowf = H2f[:, 0:JT * P]
        t128f, jcolf, hmf = rhT[:, 0:48], rhT[:, 48:55], rhT[:, 56:72]
        tcol, bvec, al = rhT[:, 72:79], rhT[:, 80:81], rhT[:, 96:128]
        hmm = rhT[:, 128:144]
        Mf = M[:, :, :, :].rearrange("p a b c -> p (a b c)")
        ck = Mf[0:112, 0:7 * 48].rearrange("p (c t) -> p c t", c=7)
        a12 = Mf[:, 1300:1300 + NT * 16].rearrange("p (t k) -> p t k", k=16)
        amax = H2f[:, 304:304 + NT * HEADS].rearrange("p (t k) -> p t k", k=HEADS)
        mv0 = H2f[:, 0:6 * NT].rearrange("p (k t) -> p k t", t=NT)
        st60 = XT[:, 1, 0:6 * NT].rearrange("p (t k) -> p t k", k=6)
        cmp2 = Mf[0:48, 512:512 + JT * P]
        wt_sb = ST[:, 0, :, :]
        trow_i = ti32[0:1, 1112:1112 + JT * P]
        tq = rhT[0:1, 144:144 + FWIN + 1].bitcast(i32)
        ringf = ring[:, :, :].rearrange("p a b -> p (a b)")
        er = ringf[:, 0:JT * 2 * P].bitcast(i32).rearrange("p (c e) -> p c e", c=JT)
        erf = ringf[:, 2048:2048 + JT * 2 * P].rearrange("p (c e) -> p c e", c=JT)
        hsb = sb("hsb", [P, 2, AW])
        hst = XN
        gtT = hsb[0:8, :, :].rearrange("p a b -> p (a b)")[:, 0:GT_ * P]
        XT0 = XT[:, 0, :].rearrange("p (a b) -> p a b", a=2)

        flat = lambda t: t[:, :, :, :].rearrange("p a b c -> p (a b c)")
        fw1 = flat(ew[0])[:, 0:KD * HF].rearrange("p (c n) -> p c n", c=KD)
        fw2 = flat(ew[1])[:, 0:HF // P * D].rearrange("p (c n) -> p c n", n=D)
        ew2f = flat(ew[2])
        hid = [flat(H1)[:, m * 512:(m + 1) * 512] for m in range(4)] + [H2f[:, m * 512:(m + 1) * 512] for m in range(2)] \
            + [ew2f[:, m * 512:(m + 1) * 512] for m in range(2)]
        yst = ew2f[:, 1024:2048].rearrange("p (t d) -> p t d", d=D)
        yo = ew2f[:, 2048:3072].rearrange("p (t d) -> p t d", d=D)
        fb2 = bias0
        fb1 = sb("fb1", [P, HF // P])
        wr = sb("wr", [P, KD])
        br = sb("br", [P, 1])
        wtok = sb("wtok", [P, NT])
        NCH = (NG * GT_) // GT_
        RCH = RING * W // GT_
        yin2 = flat(ew[0])[:, 0:(NT - RCH * GT_) * D].rearrange("p (t d) -> p t d", d=D)
        jint = sb("jint", [P, 15], i32)
        cand, cmsk = ti32[:, 0:15], ti32[:, 16:31]
        tbits, nbi, tauf = ti32[:, 32:33], ti32[:, 33:34], ti32[:, 34:35]
        H1f = flat(H1)
        key, vmask = H1f[:, 64:64 + NT], H1f[:, 116:118]
        cnt, ge, nb = H1f[:, 120:135], H1f[:, 136:151], H1f[:, 152:153]
        tie = H1f[:, 160:160 + NT + 1]
        gt = H1f[:, 212:212 + NT]
        incl, rank, mask = H1f[:, 264:264 + NT], H1f[:, 316:316 + NT], H1f[:, 368:368 + NT]
        tri = H1f[:, 512:512 + P]
        cmp3 = H2f[:, 0:15 * NT].rearrange("p (j t) -> p j t", j=15)

        banks = [ctx.enter_context(nc.psum_tensor(f"bank{i}", [P, 512], f32)) for i in range(8)]
        trB, e2B, agB, wkB = banks[0], banks[1], banks[2:4], banks[4:8]

        names = """iotas consts lasts wload x_in small_in weights_in edge_rows edge_want rank_in rank_ps walk_in walk_ps
        erf_in idx_ps tables wt_ps wt_in wal_ps wext_in var0 sq0 nmr0 xn0 xt0 p0tr p0mm p0ev attn_want
        gmax_in gmax_out shift_in rows_ready s_ready st_ready tr_done e2_done e_ready exp_done m_ready
        agg_done acc_done pe_items act_items dve_items ln_var ln_sq ln_nmr ln_xn exp_in exp_out hst_out
        dve_pro dve_fr dve_gr act_tick dve_tick pool_tick pe_tick sp_tick gate_in out_dma tokens zeroed
        b_s_ready b_agg_done b_acc_done b_pe_items b_act_items b_dve_items b_ln_var b_ln_sq b_ln_nmr b_ln_xn b_yst b_yo b_ydma
        b_gr b_weights b_fin y_in key_ok cnt_in
        cnt_ps tie_ps tie_in fin_in fin_out fin_free""".split()
        s = {n: sem(n) for n in names}
        gs = [sem(f"rows{r}") for r in range(RING)]
        isem = [sem(f"indices{r}") for r in range(RING)]
        hs_dma = [sem("hs_dma0"), sem("hs_dma1")]
        block = ctx.enter_context(nc.Block())

        class Steps:

            def __init__(self, eng, name, base=0):
                self.eng, self.sem, self.base, self.n = eng, s[name], base, 0

            def did(self, ins):
                self.n += 1
                ins.then_inc(self.sem, 1)
                return self.n

            def need(self, n=None):
                n = self.n if n is None else n
                self.eng.wait_ge(self.sem, self.base + n)

        def hold(eng, tick):
            eng.sem_inc(s[tick], 1)

        full_moe, full_ffn = moe_order(GT_), ffn_order(GT_)

        def vector_program(dve):
            V = nc.vector
            st = Steps(dve, "dve_pro")
            st.did(V.memset(ones[:, :], 1.0))
            st.did(V.memset(zero[:, :], 0.0))
            st.did(V.memset(acc[:, :, :], 0.0))
            st.did(V.memset(gate[:, :, :], 0.0))
            for e in range(NX):
                st.did(V.memset(rev[:, e:e + 1], float(NX - e)))
            V.memset(X[96:P, NT - 1, :], 0.0).then_inc(s["zeroed"], 1)
            dve.wait_ge(s["iotas"], 7)
            st.did(V.tensor_copy(iotaf[:, :], iota_i))
            st.did(V.tensor_copy(jrowf, jrow_i))
            st.did(V.tensor_copy(pidf[:, :], pid_i))
            st.did(V.tensor_copy(t128f, t128_i))
            st.did(V.tensor_copy(jcolf, jcol_i))
            st.did(V.tensor_copy(hmf, hm_i))
            st.need()
            V.tensor_scalar(ident[:, :], iotaf[:, :], pidf[:, 0:1], None, ALU.is_equal).then_inc(s["consts"], 1)
            st.did(V.tensor_scalar(hmm, hmf, float(C), None, ALU.is_lt))
            st.need()
            st.did(V.scalar_tensor_tensor(hmm, hmf, 0.0, hmm, ALU.is_ge, ALU.mult))
            dve.wait_ge(s["small_in"], 16 * 2)
            st.need()
            for c in range(KD):
                for side in range(2):
                    st.did(V.tensor_scalar(al[:, 16 * c + 8 * side:16 * c + 8 * side + 8], hmm[:, 8 * c:8 * c + 8],
                                           attn[:, 2 * side + c:2 * side + c + 1], None, ALU.mult))
            dve.wait_ge(s["wt_ps"], 1)
            st.need()
            V.tensor_copy(wt_sb, wkB[0][:, :].rearrange("p (a b) -> p a b", a=4)).then_inc(s["wt_in"], 1)
            dve.wait_ge(s["wal_ps"], 1)
            V.tensor_copy(wext[:, :, D:D + 16],
                          wkB[1][:, 0:32].rearrange("p (a b) -> p a b", a=2)).then_inc(s["wext_in"], 1)
            st.did(V.tensor_copy(lastf[:, :], last[:, :]))
            st.need()
            for c in range(7):
                i = V.tensor_scalar(ck[:, c, :], t128f[0:112, :], lastf[:, c:c + 1], None, ALU.is_gt)
            i.then_inc(s["rank_in"], 1)
            dve.wait_ge(s["rank_ps"], 1)
            st.did(V.tensor_scalar(bvec[0:48, :], banks[0][0:48, 0:1], pidf[0:48, 0:1], 1.0, ALU.add, ALU.add))
            st.need()
            V.tensor_scalar(cmp2, jrowf[0:48, :], bvec[0:48, 0:1], None, ALU.is_ge).then_inc(s["walk_in"], 1)
            dve.wait_ge(s["walk_ps"], 1)
            st.did(V.tensor_copy(trow_i[0:1, 0:512], banks[1][0:1, :]))
            st.did(V.tensor_copy(trow_i[0:1, 512:JT * P], banks[2][0:1, 0:JT * P - 512]))
            st.did(V.tensor_copy(tcol, banks[3][:, 0:7]))
            st.need()
            st.did(V.tensor_copy(tab[0:1, :, 0:4], trow_i[0:1, 0:4 * FWIN].rearrange("o (w u) -> o w u", u=4)))
            st.did(V.tensor_scalar(tq[0:1, :], trow_i[0:1, 0:4 * FWIN + 4].rearrange("o (w u) -> o w u", u=4)[:, :, 0],
                                   2, None, ALU.logical_shift_right))
            st.did(V.tensor_tensor(jcolf, jcolf, tcol, ALU.subtract))
            st.need()
            st.did(V.tensor_scalar(tab[0:1, :, 4], tq[0:1, 0:FWIN], float(NG - 1), None, ALU.min))
            st.did(V.tensor_tensor(tab[0:1, :, 5], tq[0:1, 1:FWIN + 1], tq[0:1, 0:FWIN], ALU.subtract))
            V.tensor_scalar(kcol, jcolf, float(EROWS - 1), None, ALU.min).then_inc(s["edge_want"], 1)
            st.did(V.tensor_scalar(tcol, tcol, float(P), None, ALU.mult))
            dve.wait_ge(s["x_in"], 16 * 5)
            st.need()
            with dve.Fori(0, NT) as t:
                V.bn_stats(st60[:, ds(t, 1), :].rearrange("p a b -> p (a b)"),
                           X[:, ds(t, 1), :].rearrange("p a b -> p (a b)")).then_inc(s["var0"], 1)
            dve.wait_ge(s["var0"], NT)
            stats(dve, st, st60[:, :, :], mv0, NT)
            V.tensor_scalar(mv0[:, 4, :], mv0[:, 4, :], 1e-5, None, ALU.add).then_inc(s["var0"], 1)
            dve.wait_ge(s["sq0"], 1)
            st.did(V.reciprocal(mv0[:, 4, :], mv0[:, 5, :]))
            st.need()
            V.scalar_tensor_tensor(mv0[:, 5, :], mv0[:, 0, :], -0.5, mv0[:, 4, :], ALU.mult, ALU.mult).then_inc(s["nmr0"], 1)
            dve.sem_inc(s["xt0"], 2)

            def xt_copy(t, par):
                dve.wait_ge(s["p0tr"], t + 3)
                dve.wait_ge(s["p0mm"], t + 1)
                V.tensor_copy(XT0[:, par, :], wkB[par][:, 0:PAIR]).then_inc(s["xt0"], 1)
            with dve.Fori(0, NT // 2) as i:
                xt_copy(2 * i, 0)
                xt_copy(2 * i + 1, 1)
            xt_copy(NT - 1, 0)
            dve.wait_ge(s["p0ev"], NT + 2)
            st.did(V.tensor_reduce(mx[:, 0:8], a12[:, 0:NT - 1, 0:8].rearrange("p t h -> p h t"), axis=AX.X, op=ALU.max))
            st.did(V.tensor_reduce(mx[:, 8:16], a12[:, 0:NT - 1, 0:8].rearrange("p t h -> p h t"), axis=AX.X, op=ALU.min))
            st.need()
            st.did(V.tensor_tensor(mx[0:LASTROWS, 0:8], mx[0:LASTROWS, 0:8], a12[0:LASTROWS, NT - 1, 0:8], ALU.max))
            st.did(V.tensor_tensor(mx[0:LASTROWS, 8:16], mx[0:LASTROWS, 8:16], a12[0:LASTROWS, NT - 1, 0:8], ALU.min))
            st.need()
            V.tensor_scalar(mx[:, 8:16], mx[:, 8:16], -1.0, None, ALU.mult).then_inc(s["gmax_in"], 1)
            dve.wait_ge(s["gmax_out"], 1)
            st.did(V.tensor_copy(amax[:, :, :], mx[:, 16:24].unsqueeze(1).to_broadcast([P, NT, HEADS])))
            st.need()
            st.did(V.tensor_tensor(a2sh[:, :, 8:16], a12[:, :, 8:16], amax[:, :, :], ALU.add))
            st.did(V.tensor_copy(a2sh[:, :, 0:8], a12[:, :, 8:16]))
            st.need()
            V.scalar_tensor_tensor(a2sh[:, :, 8:16], a2sh[:, :, 8:16], 0.2, a2sh[:, :, 8:16],
                                   ALU.mult, ALU.max).then_inc(s["shift_in"], 1)
            dve.wait_ge(s["edge_rows"], 16 * JT)
            st.did(V.tensor_copy(erf[:, :, 0:P], er[:, :, 0:P]))
            for c in range(JT):
                st.did(V.tensor_scalar(erf[:, c, P:2 * P], er[:, c, P:2 * P], tcol[:, c:c + 1], None, ALU.subtract))
            st.need()
            V.memset(M[:, :, :, AW:MW], 1.0).then_inc(s["erf_in"], 1)
            dve.wait_ge(s["idx_ps"], 1)
            for h, (a, b) in enumerate(((0, 4), (4, JT))):
                w = (b - a) * P
                st.did(V.tensor_copy(idxp[:, a * P:b * P], wkB[h][:, 0:w]))
                st.did(V.tensor_copy(dloc[:, a * P:b * P], wkB[2 + h][:, 0:w]))
            st.need()
            V.memset(gate[:, :, NX:8], 0.0).then_inc(s["tables"], 1)

            if stage == 0:
                return
            dve.sem_inc(s["acc_done"], 2)

            def selection(v, par, ready, done):
                V.tensor_tensor(S[:, par, :, :], iotaf[:, :].unsqueeze(1).to_broadcast([P, W, P]),
                                dloc[:, ds(v * W, W)].unsqueeze(2).to_broadcast([P, W, P]),
                                ALU.is_equal).then_inc(ready, 1)

            def front_a(v, par, first=False):
                if not first:
                    dve.wait_ge(s["agg_done"], (v - 1) * W)
                selection(v, par, s["s_ready"], None)
                row = (v % RING) * W
                g = ring[:, ds(row, W), :]
                dve.wait_ge(s["e2_done"], v + 1)
                dve.wait_ge(s["rows_ready"], v + 1)
                V.tensor_tensor(e1[:, :, :], e2B[:, 0:W * 16].rearrange("p (w k) -> p w k", w=W)[:, :, 0:8],
                                g[:, :, D:AW], ALU.add).then_inc(s["dve_fr"], 1)
                dve.wait_ge(s["dve_fr"], 2 * v + 1)
                V.scalar_tensor_tensor(e2[:, :, :], e1[:, :, :], 0.2, e1[:, :, :],
                                       ALU.mult, ALU.max).then_inc(s["dve_fr"], 1)
                dve.wait_ge(s["dve_fr"], 2 * v + 2)
                V.tensor_tensor(e1[:, :, :], e2[:, :, :], e2B[:, 0:W * 16].rearrange("p (w k) -> p w k", w=W)[:, :, 8:16],
                                ALU.subtract).then_inc(s["e_ready"], 1)
                dve.wait_ge(s["exp_done"], v + 1)
                V.tensor_tensor(M[:, par, :, 0:D].rearrange("p w (h c) -> p w h c", c=C),
                                g[:, :, 0:D].rearrange("p w (h c) -> p w h c", c=C),
                                M[:, par, :, D:AW].unsqueeze(3).to_broadcast([P, W, HEADS, C]),
                                ALU.mult).then_inc(s["m_ready"], 1)

            def back(w, width, ts, done, accd):
                for u in range(W):
                    dve.wait_ge(done, w * W + u + 1)
                    dve.wait_ge(accd, w * W + u + 2)
                    a = acc[:, ds(ts[u] % 8, 1), 0:width].rearrange("p a b -> p (a b)")
                    V.tensor_tensor(a, a, agB[u % 2][:, 0:width], ALU.add).then_inc(accd, 1)

            def regs(eng, w, which):
                return [eng.value_load(tab[0:1, ds(w, 1), c:c + 1].rearrange("o a b -> o (a b)"), min_val=0,
                                       max_val=NT - 1 if c < 4 else (NG - 1 if c == 4 else 1)) for c in which]

            front_a(0, 0, True)
            with dve.Fori(0, NWIN // 2) as i:
                for u in range(2):
                    w = 2 * i + u
                    ts = regs(dve, w, (0, 1, 2, 3, 4, 5))
                    front_a(w + 1, 1 - u)
                    back(w, MW, ts, s["agg_done"], s["acc_done"])
                    hold(dve, "dve_tick")
                    with dve.If(ts[5] > 0):
                        dve.wait_ge(s["acc_done"], w * W + W + 2)
                        finish_a_dve(dve, ts[4], GT_)
                        hold(dve, "dve_tick")
            dve.wait_ge(s["acc_done"], NWIN * W + 2)
            finish_a_dve(dve, NG, NT - NG * GT_)
            if stage > 1:
                phase_b_dve(dve, selection, back, regs)

        def stats(dve, st, src, out_, n):
            V = nc.vector
            st.did(V.tensor_tensor(out_[:, 0, 0:n], src[:, 0:n, 1], src[:, 0:n, 4], ALU.add))
            st.did(V.tensor_tensor(out_[:, 1, 0:n], src[:, 0:n, 1], src[:, 0:n, 4], ALU.subtract))
            st.did(V.tensor_tensor(out_[:, 2, 0:n], src[:, 0:n, 2], src[:, 0:n, 5], ALU.add))
            st.need()
            st.did(V.scalar_tensor_tensor(out_[:, 3, 0:n], out_[:, 1, 0:n], 0.25, out_[:, 1, 0:n], ALU.mult, ALU.mult))
            st.need()
            st.did(V.scalar_tensor_tensor(out_[:, 4, 0:n], out_[:, 2, 0:n], 1.0 / D, out_[:, 3, 0:n], ALU.mult, ALU.add))
            st.need()

        def taken(eng, it, name, pre=""):
            c, n = it.taken(name)
            eng.wait_ge(s[f"{pre}{c}_items"], n)

        def norm_dve(dve, st, T0, nt, k, group, extra, pre=""):
            V = nc.vector
            hold(dve, "dve_tick")
            for i in range(nt):
                st.did(V.bn_stats(st6[:, i, :], X[:, ds(T0 + i, 1), :].rearrange("p a b -> p (a b)")))
            st.need()
            stats(dve, st, st6[:, 0:nt, :], mv, nt)
            if not extra:
                st.did(V.memset(sq[:, GT_:2 * GT_], 1.0))
            V.tensor_scalar(sq[:, 0:nt], mv[:, 4, 0:nt], 1e-5, None, ALU.add).then_inc(s[pre + "ln_var"], 1)
            dve.wait_ge(s[pre + "ln_sq"], group * (1 if pre else 2) + k + 1)
            st.did(V.reciprocal(rc[:, :], sqr[:, :]))
            st.need()
            V.scalar_tensor_tensor(mv[:, 5, 0:nt], mv[:, 0, 0:nt], -0.5, rc[:, 0:nt],
                                   ALU.mult, ALU.mult).then_inc(s[pre + "ln_nmr"], 1)

        GC = 63

        def finish_a_dve(dve, G, nt):
            V = nc.vector
            it = Items(moe_order(nt), G, full_moe)
            st = Steps(dve, "dve_gr", G * GC)
            T0 = G * GT_
            a0 = (G % 2) * GT_
            A_ = acc[:, ds(a0, nt), :]
            Xg = X[:, ds(T0, nt), :]
            dve.wait_ge(s["hst_out"], 16 * G)
            st.did(V.tensor_scalar(rden[:, 0:nt, :], A_[:, :, D:AW], 1e-37, None, ALU.max))
            st.did(V.tensor_scalar(sq[:, GT_:GT_ + nt], A_[:, :, AW], 1.0, None, ALU.max))
            if nt < GT_:
                st.did(V.memset(sq[:, nt:GT_], 1.0))
                st.did(V.memset(sq[:, GT_ + nt:2 * GT_], 1.0))
            st.did(V.tensor_scalar(ind[:, 0:nt], A_[:, :, AW], 1.0, None, ALU.min))
            st.need()
            st.did(V.reciprocal(rden[:, 0:nt, :], rden[:, 0:nt, :]))
            st.need()
            st.did(V.tensor_tensor(XN[:, 0:nt, :].rearrange("p t (h c) -> p t h c", c=C),
                                   A_[:, :, 0:D].rearrange("p t (h c) -> p t h c", c=C),
                                   rden[:, 0:nt, :].unsqueeze(3).to_broadcast([P, nt, HEADS, C]), ALU.mult))
            st.need()
            st.did(V.tensor_tensor(XN[:, 0:nt, :], XN[:, 0:nt, :], bias0[:, :].unsqueeze(1).to_broadcast([P, nt, D]), ALU.add))
            st.did(V.tensor_copy(A_, zero[:, 0:1].unsqueeze(2).to_broadcast([P, nt, MW])))
            st.need()
            st.did(V.tensor_tensor(Xg, Xg, XN[:, 0:nt, :], ALU.add))
            st.need()
            norm_dve(dve, st, T0, nt, 0, G, True)
            st.did(V.tensor_tensor(dinv[:, ds(T0, nt)], rc[:, GT_:GT_ + nt], ind[:, 0:nt], ALU.mult))
            nn = nt * P

            def take(name):
                dve.wait_ge(s["pe_items"], it.made(name))
                return wkB[it.at[name] % 4]

            def give(ins):
                ins.then_inc(s["dve_items"], 1)
            give(V.tensor_copy(XT[:, 1, 0:nn], take("xt1")[:, 0:nn]))

            def relu(name, buf, layer, e):
                give(V.tensor_scalar(buf[:, 1, 0:nn], take(name)[:, 0:nn], eb[:, layer, e, 1:2], 0.0, ALU.add, ALU.max))
            for name, who in it.order[3:]:
                if who != "dve":
                    continue
                kind = name.split("_")
                if kind[0] == "h1":
                    e = int(kind[1])
                    relu(name, H1[:, e % 2, :, :], 0, e)
                elif kind[0] == "h2":
                    relu(name, H2[:, :, :], 1, int(kind[1]))
                elif name == "lg":
                    ps = take(name)
                    st.did(V.tensor_tensor(rt[:, 0, 0:nt, :], ps[:, 0:nt * 8].rearrange("p (t k) -> p t k", k=8)[:, :, 0:NX],
                                           rb2[:, :].unsqueeze(1).to_broadcast([P, nt, NX]), ALU.add))
                    st.need()
                    give(V.tensor_reduce(rs[:, 0, 0:nt], rt[:, 0, 0:nt, :], axis=AX.X, op=ALU.max))
                    router(dve, st, nt, G)
                elif kind[0] in ("o", "b3"):
                    ps = take(name)
                    h = int(kind[-1])
                    for i in range(2 * h, min(nt, 2 * h + 2)):
                        st.need()
                        xi = X[:, ds(T0 + i, 1), :].rearrange("p a b -> p (a b)")
                        p_ = ps[:, (i % 2) * D:(i % 2) * D + D]
                        if kind[0] == "o":
                            e = int(kind[1])
                            ins = V.scalar_tensor_tensor(xi, p_, gate[:, i, e:e + 1], xi, ALU.mult, ALU.add)
                        else:
                            ins = V.tensor_tensor(xi, xi, p_, ALU.add)
                        if i == min(nt, 2 * h + 2) - 1:
                            give(ins)
                            dve.wait_ge(s["dve_items"], it.taken(name)[1])
                        else:
                            st.did(ins)
                elif name == "xu1":
                    norm_dve(dve, st, T0, nt, 1, G, True)
                    give(V.tensor_copy(XT[:, 1, 0:nn], take(name)[:, 0:nn]))
            assert nt < GT_ or st.n == GC, st.n

        def router(dve, st, nt, G):
            V = nc.vector
            r = lambda k: rt[:, k, 0:nt, :]
            q = lambda k: rs[:, k, 0:nt]
            bc = lambda a: a.unsqueeze(2).to_broadcast([P, nt, NX])
            rv = rev[:, :].unsqueeze(1).to_broadcast([P, nt, NX])

            def do(ins):
                st.did(ins)
                st.need()
            dve.wait_ge(s["dve_items"], Items(moe_order(nt), G, full_moe).taken("lg")[1])
            V.tensor_tensor(r(0), r(0), bc(q(0)), ALU.subtract).then_inc(s["exp_in"], 1)
            dve.wait_ge(s["exp_out"], 2 * G + 1)
            do(V.tensor_reduce(q(1), r(1), axis=AX.X, op=ALU.add))
            do(V.reciprocal(q(1), q(1)))
            do(V.tensor_tensor(r(1), r(1), bc(q(1)), ALU.mult))

            def top(src, val, hot, tmp):
                do(V.tensor_reduce(q(val), r(src), axis=AX.X, op=ALU.max))
                do(V.tensor_tensor(r(tmp), r(src), bc(q(val)), ALU.is_equal))
                do(V.tensor_tensor(r(tmp), r(tmp), rv, ALU.mult))
                do(V.tensor_reduce(q(7), r(tmp), axis=AX.X, op=ALU.max))
                do(V.tensor_tensor(r(hot), r(tmp), bc(q(7)), ALU.is_equal))
            top(1, 2, 2, 3)
            do(V.scalar_tensor_tensor(r(4), r(2), -2.0, r(1), ALU.mult, ALU.add))
            top(4, 3, 5, 3)
            V.tensor_tensor(q(3), q(3), q(2), ALU.subtract).then_inc(s["exp_in"], 1)
            dve.wait_ge(s["exp_out"], 2 * G + 2)
            do(V.tensor_scalar(q(5), q(4), 1.0, None, ALU.add))
            do(V.reciprocal(q(5), q(5)))
            do(V.tensor_tensor(q(6), q(4), q(5), ALU.mult))
            do(V.tensor_tensor(r(2), r(2), bc(q(5)), ALU.mult))
            do(V.tensor_tensor(r(5), r(5), bc(q(6)), ALU.mult))
            V.tensor_tensor(gate[:, 0:nt, 0:NX], r(2), r(5), ALU.add).then_inc(s["gate_in"], 1)
            dve.wait_ge(s["gate_in"], G + 1)

        GB = 16

        def finish_b_dve(dve, G, nt):
            V = nc.vector
            it = Items(ffn_order(nt), G, full_ffn)
            st = Steps(dve, "b_gr", G * GB)
            T0, nn = G * GT_, nt * P
            A_ = acc[:, ds((G % 2) * GT_, nt), 0:D]
            for i in range(nt):
                xi = X[:, ds(T0 + i, 1), :].rearrange("p a b -> p (a b)")
                st.did(V.scalar_tensor_tensor(xi, acc[:, ds((G % 2) * GT_ + i, 1), 0:D].rearrange("p a b -> p (a b)"),
                                              dinv[:, ds(T0 + i, 1)], xi, ALU.mult, ALU.add))
            st.need()
            hold(dve, "dve_tick")
            st.did(V.tensor_copy(A_, zero[:, 0:1].unsqueeze(2).to_broadcast([P, nt, D])))
            norm_dve(dve, st, T0, nt, 0, G, True, "b_")
            dve.wait_ge(s["b_ln_xn"], G + 1)
            Xg = X[:, ds(T0, nt), :]
            st.did(V.tensor_tensor(Xg, Xg, XN[:, 0:nt, :], ALU.add))

            def take(name):
                dve.wait_ge(s["b_pe_items"], it.made(name))
                return wkB[it.at[name] % 4]

            def give(ins):
                ins.then_inc(s["b_dve_items"], 1)
            give(V.tensor_copy(XT[:, 1, 0:nn], take("xt1")[:, 0:nn]))
            give(V.tensor_scalar(wtok[:, ds(T0, nt)], take("wt")[:, 0:nt], br[:, 0:1], None, ALU.add))
            for h in range(2 if nt > 2 else 1):
                ps = take(f"y_{h}")
                m = min(2, nt - 2 * h)
                give(V.tensor_tensor(yst[:, 2 * h:2 * h + m, :], ps[:, 0:m * D].rearrange("p (t d) -> p t d", d=D),
                                     fb2[:, :].unsqueeze(1).to_broadcast([P, m, D]), ALU.add))
            dve.wait_ge(s["b_dve_items"], it.taken(it.order[-1][0])[1])
            dve.sem_inc(s["b_yst"], 1)
            st.need()
            assert nt < GT_ or st.n == GB, st.n

        def phase_b_dve(dve, selection, back, regs):
            V = nc.vector
            dve.sem_inc(s["b_acc_done"], 2)
            selection(0, 0, s["b_s_ready"], None)
            with dve.Fori(0, NWIN // 2) as i:
                for u in range(2):
                    w = 2 * i + u
                    ts = regs(dve, w, (0, 1, 2, 3, 4, 5))
                    dve.wait_ge(s["b_agg_done"], w * W)
                    selection(w + 1, 1 - u, s["b_s_ready"], None)
                    back(w, D, ts, s["b_agg_done"], s["b_acc_done"])
                    hold(dve, "dve_tick")
                    with dve.If(ts[5] > 0):
                        dve.wait_ge(s["b_acc_done"], w * W + W + 2)
                        finish_b_dve(dve, ts[4], GT_)
                        hold(dve, "dve_tick")
            dve.wait_ge(s["b_acc_done"], NWIN * W + 2)
            finish_b_dve(dve, NG, NT - NG * GT_)
            last_pass_dve(dve)

        def last_pass_dve(dve):
            V = nc.vector
            st = Steps(dve, "b_fin")

            def do(ins):
                st.did(ins)
                st.need()
            dve.wait_ge(s["b_pe_items"], Items(ffn_order(NT - NG * GT_), NG, full_ffn).made("y_0"))
            do(V.memset(tbits, 0))
            do(V.tensor_scalar(tri, iotaf[:, :], pidf[:, 0:1], None, ALU.is_gt))
            do(V.tensor_scalar(vmask[:, 0:1], pidf[:, 0:1], float(LASTROWS), None, ALU.is_lt))
            do(V.tensor_scalar(vmask[:, 1:2], vmask[:, 0:1], 3e38, -3e38, ALU.mult, ALU.add))
            do(V.tensor_copy(key, wtok[:, :]))
            do(V.tensor_scalar(key[:, NT - 1:NT], key[:, NT - 1:NT], vmask[:, 0:1], vmask[:, 1:2], ALU.mult, ALU.add))

            def as_float(dst, bits, msk):
                do(V.tensor_scalar(msk, bits, 31, None, ALU.arith_shift_right))
                do(V.tensor_scalar(msk, msk, -1, -2147483648, ALU.bitwise_xor, ALU.bitwise_or))
                do(V.tensor_tensor(dst, bits, msk, ALU.bitwise_xor))
            for r in range(8):
                sh = 28 - 4 * r
                do(V.tensor_scalar(cand, jint[:, :], sh, None, ALU.logical_shift_left))
                do(V.tensor_tensor(cand, cand, tbits.to_broadcast([P, 15]), ALU.bitwise_or))
                as_float(cand, cand, cmsk)
                do(V.tensor_tensor(cmp3, key.unsqueeze(1).to_broadcast([P, 15, NT]),
                                   cand.bitcast(f32).unsqueeze(2).to_broadcast([P, 15, NT]), ALU.is_ge))
                V.tensor_reduce(cnt, cmp3, axis=AX.X, op=ALU.add).then_inc(s["cnt_in"], 1)
                dve.wait_ge(s["cnt_ps"], r + 1)
                do(V.tensor_scalar(ge, banks[0][:, 0:15], float(CAP), None, ALU.is_ge))
                do(V.tensor_reduce(nb, ge, axis=AX.X, op=ALU.add))
                do(V.tensor_copy(nbi, nb))
                do(V.tensor_scalar(nbi, nbi, sh, None, ALU.logical_shift_left))
                do(V.tensor_tensor(tbits, tbits, nbi, ALU.bitwise_or))
            as_float(tauf, tbits, cmsk[:, 0:1])
            tau = tauf.bitcast(f32)
            do(V.tensor_scalar(gt, key, tau, None, ALU.is_gt))
            do(V.tensor_scalar(tie[:, 1:NT + 1], key, tau, None, ALU.is_equal))
            V.tensor_reduce(tie[:, 0:1], gt, axis=AX.X, op=ALU.add).then_inc(s["tie_in"], 1)
            dve.wait_ge(s["tie_ps"], 1)
            do(V.tensor_tensor_scan(incl, ones[:, 0:NT], banks[0][:, 1:NT + 1], 0.0, ALU.mult, ALU.add))
            do(V.tensor_tensor(rank, incl, banks[0][:, 1:NT + 1], ALU.subtract))
            do(V.tensor_tensor(rank, rank, banks[1][:, 0:NT], ALU.add))
            do(V.tensor_scalar(nb, banks[0][:, 0:1], -1.0, float(CAP), ALU.mult, ALU.add))
            do(V.tensor_scalar(rank, rank, nb, None, ALU.is_lt))
            do(V.tensor_tensor(rank, rank, tie[:, 1:NT + 1], ALU.mult))
            do(V.tensor_tensor(mask, gt, rank, ALU.add))
            dve.wait_ge(s["y_in"], 16 * 2)
            hold(dve, "dve_tick")

            def add(t, y):
                xi = X[:, ds(t, 1), :].rearrange("p a b -> p (a b)")
                return V.scalar_tensor_tensor(xi, y, mask[:, ds(t, 1)], xi, ALU.mult, ALU.add)
            with dve.Fori(0, RCH) as c:
                for i in range(GT_):
                    ins = add(c * GT_ + i, ring[:, ds(c * GT_ + i, 1), 0:D].rearrange("p a b -> p (a b)"))
                ins.then_inc(s["fin_out"], 1)
            for t in range(RCH * GT_, NT):
                ins = add(t, yin2[:, t - RCH * GT_, :])
            ins.then_inc(s["fin_out"], 1)

        def gpsimd_program(pool):
            g = nc.gpsimd
            g.iota(iota_i, pattern=[[1, P]], base=0, channel_multiplier=0).then_inc(s["iotas"], 1)
            g.iota(jrow_i, pattern=[[1, JT * P]], base=0, channel_multiplier=0).then_inc(s["iotas"], 1)
            g.iota(pid_i, pattern=[[1, 1]], base=0, channel_multiplier=1).then_inc(s["iotas"], 1)
            g.iota(t128_i, pattern=[[P, 48]], base=P, channel_multiplier=0).then_inc(s["iotas"], 1)
            g.iota(jcol_i, pattern=[[P, 7]], base=0, channel_multiplier=1).then_inc(s["iotas"], 1)
            g.iota(hm_i, pattern=[[P, 2], [-C, HEADS]], base=0, channel_multiplier=1).then_inc(s["iotas"], 1)
            g.iota(jint[:, :], pattern=[[1, 15]], base=1, channel_multiplier=0).then_inc(s["iotas"], 1)
            pool.wait_ge(s["edge_want"], 1)
            for c in range(JT):
                g.indirect_dma_start(out=er[:, c, :], out_offset=None, in_=A["edges"][:, :],
                                     in_offset=bass.IndirectOffsetOnAxis(ap=kcol[:, c:c + 1], axis=0)
                                     ).then_inc(s["edge_rows"], 16)
            pool.wait_ge(s["gmax_in"], 1)
            g.partition_all_reduce(mx[:, 16:32], mx[:, 0:16], P, bass.bass_isa.ReduceOp.max).then_inc(s["gmax_out"], 1)
            pool.wait_ge(hs_dma[0], 16 * (NT - NT // 2))
            pool.wait_ge(hs_dma[1], 16 * (NT // 2))
            pool.wait_ge(s["tables"], 1)

            def gather(table, width, r, it_, base, used):
                pool.wait_ge(isem[r], 16 * (it_ + base + 1))
                if used is not None:
                    pool.wait_ge(*used)
                hold(pool, "pool_tick")
                for u in range(W):
                    o = ring[:, r * W + u, 0:width]
                    g.indirect_dma_start(out=o, out_offset=None, in_=table[:, :],
                                         in_offset=bass.IndirectOffsetOnAxis(ap=idxs[:, r, u:u + 1], axis=0)
                                         ).then_inc(gs[r], 16)
            if stage == 0:
                return
            for r in range(RING):
                gather(ht0, AW, r, 0, 0, None)
            with pool.Fori(1, FWIN // RING) as k:
                for r in range(RING):
                    gather(ht0, AW, r, k, 0, (s["m_ready"], (k - 1) * RING + r + 1))
            if stage == 1:
                return
            pool.wait_ge(s["hst_out"], 16 * (NG + 1))
            for r in range(RING):
                gather(ht1, D, r, 0, FWIN // RING, (s["m_ready"], FWIN))
            with pool.Fori(1, FWIN // RING) as k:
                for r in range(RING):
                    gather(ht1, D, r, k, FWIN // RING, (s["b_agg_done"], ((k - 1) * RING + r + 1) * W))

        def sync_program(sp):
            sp.dma_start(last[:, :], A["last"][:, :]).then_inc(s["small_in"], 16)
            sp.dma_start(attn[:, :], A["attn"][:, :]).then_inc(s["small_in"], 16)
            sp.dma_start(wext[:, :, 0:D], A["w0"].rearrange("p (c n) -> p c n", c=KD)).then_inc(s["wload"], 16)
            for q in range(4):
                n = (NT - 1) // 4
                sp.dma_start(X[:, q * n:q * n + n, :],
                             A["x"][q * n * P:(q + 1) * n * P, :].rearrange("(t p) d -> p t d", p=P)
                             ).then_inc(s["x_in"], 16)
            sp.wait_ge(s["zeroed"], 1)
            sp.dma_start(X[0:LASTROWS, NT - 1, :], A["x"][(NT - 1) * P:N, :]).then_inc(s["x_in"], 16)
            sp.dma_start(bias0[:, :], A["bias0"].to_broadcast([P, D])).then_inc(s["weights_in"], 16)
            for i in range(3):
                sp.dma_start(ew[i][:, :, :, :].rearrange("p a b c -> p (a b c)"), A[f"ew{i}"][:, :]).then_inc(s["weights_in"], 16)
            for dst, src in ((eb[:, :, :, :].rearrange("p a b c -> p (a b c)"), A["eb"][:, :]), (eb3[:, :], A["eb3"][:, :]),
                             (rw1[:, :, :].rearrange("p a b -> p (a b)"), A["rw1"][:, :]), (rb1[:, :], A["rb1"][:, :]),
                             (rw2[:, :], A["rw2"][:, :]), (rb2[:, :], A["rb2"].to_broadcast([P, NX])),
                             (w1g[:, :, :].rearrange("p a b -> p (a b)"), A["w1g"][:, :])):
                sp.dma_start(dst, src).then_inc(s["weights_in"], 16)

            def store(t, par):
                sp.wait_ge(s["p0ev"], t + 3)
                sp.dma_start(ht0[ds(t * P, P), :], hsb[:, par, :]).then_inc(hs_dma[par], 16)
            with sp.Fori(0, NT // 2) as i:
                store(2 * i, 0)
                store(2 * i + 1, 1)
            store(NT - 1, 0)
            if stage == 0:
                sp.wait_ge(s["shift_in"], 1)
                sp.wait_ge(s["tables"], 1)
                sp.wait_ge(hs_dma[0], 16 * 25)
                sp.wait_ge(hs_dma[1], 16 * 24)
                sp.wait_ge(s["weights_in"], 16 * 11)
                dbg_(sp)
                return
            sp.wait_ge(s["tables"], 1)
            sp.wait_ge(s["shift_in"], 1)
            for r in range(RING):
                sp.dma_start(idxs[:, r, :], idxp[:, r * W:(r + 1) * W]).then_inc(isem[r], 16)

            def relay(k, r, base, more):
                sp.wait_ge(gs[r], 16 * W * (k + base + 1))
                sp.sem_inc(s["rows_ready"], 1)
                if more:
                    sp.dma_start(idxs[:, r, :], idxp[:, ds(((k + 1) * RING + r) * W, W)]).then_inc(isem[r], 16)
            with sp.Fori(0, FWIN // RING - 1) as k:
                for r in range(RING):
                    relay(k, r, 0, True)
            for r in range(RING):
                relay(FWIN // RING - 1, r, 0, False)
            if stage > 1:
                sp.wait_ge(s["hst_out"], 16 * (NG + 1))
                sp.dma_start(fw1.rearrange("p a b -> p (a b)"), A["fw1"][:, :]).then_inc(s["b_weights"], 16)
                sp.dma_start(fw2.rearrange("p a b -> p (a b)"), A["fw2"][:, :]).then_inc(s["b_weights"], 16)
                for dst, src in ((fb1[:, :], A["fb1"][:, :]), (fb2[:, :], A["fb2"].to_broadcast([P, D])),
                                 (wr[:, :], A["wr"][:, :]), (br[:, :], A["br"].to_broadcast([P, 1]))):
                    sp.dma_start(dst, src).then_inc(s["b_weights"], 16)
                for r in range(RING):
                    sp.dma_start(idxs[:, r, :], idxp[:, r * W:(r + 1) * W]).then_inc(isem[r], 16)
                with sp.Fori(0, FWIN // RING - 1) as k:
                    for r in range(RING):
                        relay(k, r, FWIN // RING, True)
                for r in range(RING):
                    relay(FWIN // RING - 1, r, FWIN // RING, False)
                sp.wait_ge(s["b_ydma"], 16 * (NG + 1))
                sp.wait_ge(s["b_agg_done"], NWIN * W)
                nr = RCH * GT_
                sp.dma_start(ring[:, 0:nr, 0:D], yd[0:nr * P, :].rearrange("(t p) d -> p t d", p=P)).then_inc(s["y_in"], 16)
                sp.dma_start(yin2[:, :, :], yd[nr * P:NT * P, :].rearrange("(t p) d -> p t d", p=P)).then_inc(s["y_in"], 16)
                with sp.Fori(0, RCH) as c:
                    sp.wait_ge(s["fin_out"], c + 1)
                    sp.dma_start(out[ds(c * GT_ * P, GT_ * P), :].rearrange("(t p) d -> p t d", p=P),
                                 X[:, ds(c * GT_, GT_), :]).then_inc(s["out_dma"], 16)
                sp.wait_ge(s["fin_out"], RCH + 1)
                sp.dma_start(out[nr * P:(NT - 1) * P, :].rearrange("(t p) d -> p t d", p=P),
                             X[:, nr:NT - 1, :]).then_inc(s["out_dma"], 16)
                sp.dma_start(out[(NT - 1) * P:N, :], X[0:LASTROWS, NT - 1, :]).then_inc(s["out_dma"], 16)
                sp.wait_ge(s["out_dma"], 16 * (RCH + 2))
            if stage == 1:
                sp.wait_ge(s["hst_out"], 16 * (NG + 1))
                sp.wait_ge(s["tokens"], 1)
                sp.dma_start(out[0:(NT - 1) * P, :].rearrange("(t p) d -> p t d", p=P), X[:, 0:NT - 1, :]).then_inc(s["out_dma"], 16)
                sp.dma_start(out[(NT - 1) * P:N, :], X[0:LASTROWS, NT - 1, :]).then_inc(s["out_dma"], 16)
                sp.wait_ge(s["out_dma"], 32)

        def dbg_(sp):
            sp.dma_start(out[0:P, :], idxp[:, 0:D].bitcast(f32)).then_inc(s["out_dma"], 16)
            sp.dma_start(out[P:2 * P, :], dloc[:, 0:D]).then_inc(s["out_dma"], 16)
            sp.dma_start(out[2 * P:2 * P + 1, 0:192], tab[0:1, 0:64, :].rearrange("o a b -> o (a b)").bitcast(f32)).then_inc(s["out_dma"], 16)
            sp.dma_start(out[3 * P:6 * P, :], ht0[0:3 * P, 0:256]).then_inc(s["out_dma"], 16)
            sp.dma_start(out[6 * P:7 * P, :], a2sh[:, 0:16, :].rearrange("p a b -> p (a b)")).then_inc(s["out_dma"], 16)
            sp.wait_ge(s["out_dma"], 16 * 5)


        def scalar_program(act):
            a = nc.scalar
            act.wait_ge(s["var0"], NT + 1)
            a.activation(mv0[:, 5, :], mv0[:, 4, :], ACT.Sqrt).then_inc(s["sq0"], 1)
            act.wait_ge(s["nmr0"], 1)
            hold(act, "p0ev")
            hold(act, "p0ev")

            def normalise(t, par):
                act.wait_ge(s["p0tr"], t + 1)
                hold(act, "act_tick")
                a.activation(XN[:, par, :], X[:, ds(t, 1), :].rearrange("p a b -> p (a b)"), ACT.Identity,
                             scale=mv0[:, 4, ds(t, 1)], bias=mv0[:, 5, ds(t, 1)]).then_inc(s["xn0"], 1)

            def evacuate(t, par, half):
                act.wait_ge(s["p0mm"], t + 3)
                act.wait_ge(hs_dma[par], 16 * half)
                hold(act, "act_tick")
                a.activation(hsb[:, par, :], wkB[2 + par][:, 0:AW], ACT.Copy)
                a.activation(a12[:, ds(t, 1), :].rearrange("p a b -> p (a b)"), wkB[2 + par][:, D:D + 16],
                             ACT.Copy).then_inc(s["p0ev"], 1)
            normalise(0, 0)
            with act.Fori(0, NT // 2) as i:
                for u in range(2):
                    normalise(2 * i + u + 1, 1 - u)
                    evacuate(2 * i + u, u, i)
            evacuate(NT - 1, 0, NT // 2)
            if stage == 0:
                return
            act.wait_ge(s["weights_in"], 16 * 11)

            def regs(w):
                return [act.value_load(tab[0:1, ds(w, 1), c:c + 1].rearrange("o a b -> o (a b)"), min_val=0,
                                       max_val=NG - 1 if c == 4 else 1) for c in (4, 5)]

            def front_a(v, par):
                act.wait_ge(s["tr_done"], v + 1)
                a.activation(ST[:, par, :, :].rearrange("p a b -> p (a b)"), trB[:, :], ACT.Copy).then_inc(s["st_ready"], 1)
                act.wait_ge(s["e_ready"], v + 1)
                a.activation(M[:, par, :, D:AW], e1[:, :, :], ACT.Exp).then_inc(s["exp_done"], 1)
            front_a(0, 0)
            with act.Fori(0, NWIN // 2) as i:
                for u in range(2):
                    w = 2 * i + u
                    G, ends = regs(w)
                    front_a(w + 1, 1 - u)
                    with act.If(ends > 0):
                        finish_a_act(act, G, GT_)
                        hold(act, "act_tick")
            finish_a_act(act, NG, NT - NG * GT_)
            phase_b_act(act, regs)

        def norm_act(act, T0, nt, want, pre=""):
            a = nc.scalar
            act.wait_ge(s[pre + "ln_var"], want)
            a.activation(sqr[:, :], sq[:, :], ACT.Sqrt).then_inc(s[pre + "ln_sq"], 1)
            act.wait_ge(s[pre + "ln_nmr"], want)
            hold(act, "act_tick")
            for i in range(nt):
                ins = a.activation(XN[:, i, :], X[:, ds(T0 + i, 1), :].rearrange("p a b -> p (a b)"), ACT.Identity,
                                   scale=rc[:, i:i + 1], bias=mv[:, 5, i:i + 1])
            ins.then_inc(s[pre + "ln_xn"], 1)

        def finish_a_act(act, G, nt):
            a = nc.scalar
            it = Items(moe_order(nt), G, full_moe)
            T0, nn = G * GT_, nt * P

            def take(name):
                act.wait_ge(s["pe_items"], it.made(name))
                return wkB[it.at[name] % 4]

            def give(ins):
                ins.then_inc(s["act_items"], 1)
            norm_act(act, T0, nt, 2 * G + 1)
            for name, who in it.order:
                kind = name.split("_")
                if name == "lg":
                    act.wait_ge(s["exp_in"], 2 * G + 1)
                    a.activation(rt[:, 1, 0:nt, :], rt[:, 0, 0:nt, :], ACT.Exp).then_inc(s["exp_out"], 1)
                    act.wait_ge(s["exp_in"], 2 * G + 2)
                    a.activation(rs[:, 4, 0:nt], rs[:, 3, 0:nt], ACT.Exp).then_inc(s["exp_out"], 1)
                if name == "xu0":
                    norm_act(act, T0, nt, 2 * G + 2)
                if who != "act":
                    continue
                if name in ("xt0", "xu0"):
                    give(a.activation(XT[:, 0, 0:nn], take(name)[:, 0:nn], ACT.Copy))
                elif name == "rh":
                    give(a.activation(rhT[:, 0:nn], take(name)[:, 0:nn], ACT.Relu, bias=rb1[:, 0:1]))
                elif name == "gt":
                    give(a.activation(gtT[:, 0:nn], take(name)[0:8, 0:nn], ACT.Copy))
                elif kind[0] == "h1":
                    e = int(kind[1])
                    give(a.activation(H1[:, e % 2, 0, 0:nn], take(name)[:, 0:nn], ACT.Relu, bias=eb[:, 0, e, 0:1]))
                elif kind[0] == "h2":
                    e = int(kind[1])
                    give(a.activation(H2[:, 0, 0:nn], take(name)[:, 0:nn], ACT.Relu, bias=eb[:, 1, e, 0:1]))
                elif kind[0] == "p":
                    ps, h = take(name), int(kind[1])
                    hold(act, "act_tick")
                    for i in range(2 * h, min(nt, 2 * h + 2)):
                        ins = a.activation(hst[:, i, :], ps[:, (i % 2) * D:(i % 2) * D + D], ACT.Copy,
                                           scale=dinv[:, ds(T0 + i, 1)])
                    give(ins)
            act.wait_ge(s["act_items"], it.taken(it.order[-1][0])[1])
            act.dma_start(ht1[ds(T0 * P, nn), :].rearrange("(t p) d -> p t d", p=P), hst[:, 0:nt, :]).then_inc(s["hst_out"], 16)

        def finish_b_act(act, G, nt):
            a = nc.scalar
            it = Items(ffn_order(nt), G, full_ffn)
            T0, nn = G * GT_, nt * P
            norm_act(act, T0, nt, G + 1, "b_")
            for name, who in it.order:
                if who == "act":
                    act.wait_ge(s["b_pe_items"], it.made(name))
                    ps = wkB[it.at[name] % 4][:, 0:nn]
                    if name == "xt0":
                        ins = a.activation(XT[:, 0, 0:nn], ps, ACT.Copy)
                    else:
                        m = int(name[2:])
                        ins = a.activation(hid[m][:, 0:nn], ps, ACT.Gelu_apprx_tanh, bias=fb1[:, m:m + 1])
                    ins.then_inc(s["b_act_items"], 1)
            act.wait_ge(s["b_yst"], G + 1)
            act.wait_ge(s["b_ydma"], 16 * G)
            hold(act, "act_tick")
            for i in range(nt):
                ins = a.activation(yo[:, i, :], yst[:, i, :], ACT.Copy, scale=wtok[:, ds(T0 + i, 1)])
            ins.then_inc(s["b_yo"], 1)
            act.wait_ge(s["b_yo"], G + 1)
            act.dma_start(yd[ds(T0 * P, nn), :].rearrange("(t p) d -> p t d", p=P), yo[:, 0:nt, :]).then_inc(s["b_ydma"], 16)

        def phase_b_act(act, regs):
            if stage == 1:
                hold(act, "tokens")
                return
            act.wait_ge(s["b_weights"], 16 * 6)
            with act.Fori(0, NWIN) as w:
                G, ends = regs(w)
                with act.If(ends > 0):
                    finish_b_act(act, G, GT_)
                    hold(act, "act_tick")
            finish_b_act(act, NG, NT - NG * GT_)

        def tensor_program(pe):
            t_ = nc.tensor
            pe.wait_ge(s["consts"], 1)
            pe.wait_ge(s["wload"], 16)
            for c in range(KD):
                for d in range(KD):
                    ins = t_.transpose(wkB[0][:, (c * KD + d) * P:(c * KD + d + 1) * P],
                                       wext[:, d, c * P:(c + 1) * P], ident[:, :])
            ins.then_inc(s["wt_ps"], 1)
            pe.wait_ge(s["wt_in"], 1)
            for d in range(KD):
                for c in range(KD):
                    ins = t_.matmul(wkB[1][:, 16 * d:16 * d + 16], wt_sb[:, c * KD + d, :], al[:, 16 * c:16 * c + 16],
                                    start=(c == 0), stop=(c == KD - 1))
            ins.then_inc(s["wal_ps"], 1)
            pe.wait_ge(s["rank_in"], 1)
            for c in range(7):
                ins = t_.matmul(banks[0][0:48, 0:1], ck[:, c, :], ones[0:112, 0:1], start=(c == 0), stop=(c == 6))
            ins.then_inc(s["rank_ps"], 1)
            pe.wait_ge(s["walk_in"], 1)
            t_.matmul(banks[1][:, :], ones[0:48, :], cmp2[:, 0:512], start=True, stop=True)
            t_.matmul(banks[2][:, 0:JT * P - 512], ones[0:48, :], cmp2[:, 512:JT * P], start=True, stop=True)
            for c in range(JT):
                ins = t_.matmul(banks[3][:, c:c + 1], cmp2[:, c * P:(c + 1) * P], ones[0:48, 0:1], start=True, stop=True)
            ins.then_inc(s["walk_ps"], 1)
            pe.wait_ge(s["wext_in"], 1)
            for n in ("p0tr", "p0mm"):
                hold(pe, n)
                hold(pe, n)

            def transpose_tile(t, par):
                pe.wait_ge(s["xn0"], t + 1)
                pe.wait_ge(s["xt0"], t + 1)
                for c in range(KD):
                    ins = t_.transpose(wkB[par][:, c * P:(c + 1) * P], XN[:, par, c * P:(c + 1) * P], ident[:, :])
                ins.then_inc(s["p0tr"], 1)

            def project(t, par):
                pe.wait_ge(s["xt0"], t + 3)
                pe.wait_ge(s["p0ev"], t + 1)
                for c in range(KD):
                    ins = t_.matmul(wkB[2 + par][:, 0:D + 16], XT0[:, par, c * P:(c + 1) * P], wext[:, c, :],
                                    start=(c == 0), stop=(c == KD - 1))
                ins.then_inc(s["p0mm"], 1)
            transpose_tile(0, 0)
            with pe.Fori(0, NT // 2) as i:
                for u in range(2):
                    transpose_tile(2 * i + u + 1, 1 - u)
                    project(2 * i + u, u)
            project(NT - 1, 0)
            pe.wait_ge(s["erf_in"], 1)
            pe.wait_ge(s["p0ev"], NT + 2)
            for h, (b0, b1) in enumerate(((0, 4), (4, JT))):
                for side in range(2):
                    for c in range(b0, b1):
                        ins = t_.transpose(wkB[2 * side + h][:, (c - b0) * P:(c - b0 + 1) * P],
                                           erf[:, c, side * P:(side + 1) * P], ident[:, :])
            ins.then_inc(s["idx_ps"], 1)
            if stage == 0:
                return
            pe.wait_ge(s["weights_in"], 16 * 11)
            pe.wait_ge(s["shift_in"], 1)
            pe.wait_ge(s["tables"], 1)

            def regs(w, which):
                return [pe.value_load(tab[0:1, ds(w, 1), c:c + 1].rearrange("o a b -> o (a b)"), min_val=0,
                                      max_val=NT - 1 if c < 4 else (NG - 1 if c == 4 else 1)) for c in which]

            def front_a(v, par, ts):
                pe.wait_ge(s["s_ready"], v + 1)
                pe.wait_ge(s["st_ready"], v)
                for u in range(W):
                    ins = t_.transpose(trB[:, u * P:(u + 1) * P], S[:, par, u, :], ident[:, :])
                ins.then_inc(s["tr_done"], 1)
                pe.wait_ge(s["st_ready"], v + 1)
                pe.wait_ge(s["e_ready"], v)
                for u in range(W):
                    ins = t_.matmul(e2B[:, u * 16:(u + 1) * 16], ST[:, par, u, :],
                                    a2sh[:, ds(ts[u], 1), :].rearrange("p a b -> p (a b)"), start=True, stop=True)
                ins.then_inc(s["e2_done"], 1)

            def back(w, par, width, ready, done, accd, rhs):
                pe.wait_ge(ready[0], ready[1])
                for u in range(W):
                    pe.wait_ge(accd, w * W + u + 1)
                    t_.matmul(agB[u % 2][:, 0:width], S[:, par, u, :], rhs(u), start=True, stop=True).then_inc(done, 1)
            front_a(0, 0, regs(0, (0, 1, 2, 3)))
            with pe.Fori(0, NWIN // 2) as i:
                for u in range(2):
                    w = 2 * i + u
                    front_a(w + 1, 1 - u, regs(w + 1, (0, 1, 2, 3)))
                    G, ends = regs(w, (4, 5))
                    back(w, u, MW, (s["m_ready"], w + 1), s["agg_done"], s["acc_done"], lambda k: M[:, u, k, :])
                    with pe.If(ends > 0):
                        finish_a_pe(pe, G, GT_)
                        hold(pe, "pe_tick")
            finish_a_pe(pe, NG, NT - NG * GT_)
            phase_b_pe(pe, back, regs)

        def item(pe, it, name, pre=""):
            n = it.at[name]
            if n == 0:
                for c in ("act", "dve"):
                    pe.wait_ge(s[f"{pre}{c}_items"], it.group * it.totals[c])
            if n >= 4:
                taken(pe, it, it.order[n - 4][0], pre)
            return wkB[n % 4]

        def finish_a_pe(pe, G, nt):
            t_ = nc.tensor
            it = Items(moe_order(nt), G, full_moe)
            nn = nt * P

            def end(ins):
                ins.then_inc(s["pe_items"], 1)
            for name, _ in it.order:
                kind = name.split("_")
                if name == "xt0":
                    pe.wait_ge(s["ln_xn"], 2 * G + 1)
                if name == "xu0":
                    pe.wait_ge(s["ln_xn"], 2 * G + 2)
                ps = item(pe, it, name)
                if name[:2] in ("xt", "xu"):
                    c = int(name[2])
                    for i in range(nt):
                        ins = t_.transpose(ps[:, i * P:(i + 1) * P], XN[:, i, c * P:(c + 1) * P], ident[:, :])
                elif name == "rh":
                    taken(pe, it, "xt0")
                    taken(pe, it, "xt1")
                    for c in range(KD):
                        ins = t_.matmul(ps[:, 0:nn], rw1[:, c, :], XT[:, c, 0:nn], start=(c == 0), stop=(c == KD - 1))
                elif name == "lg":
                    taken(pe, it, "rh")
                    for i in range(nt):
                        ins = t_.matmul(ps[:, i * 8:i * 8 + NX], rhT[:, i * P:(i + 1) * P], rw2[:, :], start=True, stop=True)
                elif kind[0] == "h1":
                    e, m = int(kind[1]), int(kind[2])
                    for c in range(KD):
                        ins = t_.matmul(ps[:, 0:nn], ew[0][:, e, c, m * P:(m + 1) * P], XT[:, c, 0:nn],
                                        start=(c == 0), stop=(c == KD - 1))
                elif kind[0] == "h2":
                    e, m = int(kind[1]), int(kind[2])
                    taken(pe, it, f"h1_{e}_0")
                    taken(pe, it, f"h1_{e}_1")
                    for c in range(KD):
                        ins = t_.matmul(ps[:, 0:nn], ew[1][:, e, c, m * P:(m + 1) * P], H1[:, e % 2, c, 0:nn],
                                        start=(c == 0), stop=(c == KD - 1))
                elif kind[0] == "o":
                    e, h = int(kind[1]), int(kind[2])
                    taken(pe, it, f"h2_{e}_0")
                    taken(pe, it, f"h2_{e}_1")
                    for i in range(2 * h, min(nt, 2 * h + 2)):
                        for c in range(KD):
                            ins = t_.matmul(ps[:, (i % 2) * D:(i % 2) * D + D], H2[:, c, i * P:(i + 1) * P],
                                            ew[2][:, e, c, :], start=(c == 0), stop=(c == KD - 1))
                elif name == "gt":
                    pe.wait_ge(s["gate_in"], G + 1)
                    for i in range(nt):
                        ins = t_.transpose(ps[0:8, i * P:(i + 1) * P], gate[:, i, :], ident[:, :])
                elif kind[0] == "b3":
                    taken(pe, it, "gt")
                    h = int(kind[1])
                    for i in range(2 * h, min(nt, 2 * h + 2)):
                        ins = t_.matmul(ps[:, (i % 2) * D:(i % 2) * D + D], gtT[0:NX, i * P:(i + 1) * P], eb3[:, :],
                                        start=True, stop=True)
                elif kind[0] == "p":
                    taken(pe, it, "xu0")
                    taken(pe, it, "xu1")
                    h = int(kind[1])
                    for i in range(2 * h, min(nt, 2 * h + 2)):
                        for c in range(KD):
                            ins = t_.matmul(ps[:, (i % 2) * D:(i % 2) * D + D], XT[:, c, i * P:(i + 1) * P],
                                            w1g[:, c, :], start=(c == 0), stop=(c == KD - 1))
                end(ins)

        def finish_b_pe(pe, G, nt):
            t_ = nc.tensor
            it = Items(ffn_order(nt), G, full_ffn)
            nn = nt * P
            for name, _ in it.order:
                if name == "xt0":
                    pe.wait_ge(s["b_ln_xn"], G + 1)
                ps = item(pe, it, name, "b_")
                if name[:2] == "xt":
                    c = int(name[2])
                    for i in range(nt):
                        ins = t_.transpose(ps[:, i * P:(i + 1) * P], XN[:, i, c * P:(c + 1) * P], ident[:, :])
                elif name == "wt":
                    taken(pe, it, "xt0", "b_")
                    taken(pe, it, "xt1", "b_")
                    for i in range(nt):
                        for c in range(KD):
                            ins = t_.matmul(ps[:, i:i + 1], XT[:, c, i * P:(i + 1) * P], wr[:, c:c + 1],
                                            start=(c == 0), stop=(c == KD - 1))
                elif name[0] == "h":
                    m = int(name[2:])
                    for c in range(KD):
                        ins = t_.matmul(ps[:, 0:nn], fw1[:, c, m * P:(m + 1) * P], XT[:, c, 0:nn],
                                        start=(c == 0), stop=(c == KD - 1))
                else:
                    h = int(name[2:])
                    for i in range(2 * h, min(nt, 2 * h + 2)):
                        for m in range(HF // P):
                            if i == 0:
                                taken(pe, it, f"h_{m}", "b_")
                            ins = t_.matmul(ps[:, (i % 2) * D:(i % 2) * D + D], hid[m][:, i * P:(i + 1) * P],
                                            fw2[:, m, :], start=(m == 0), stop=(m == HF // P - 1))
                ins.then_inc(s["b_pe_items"], 1)

        def phase_b_pe(pe, back, regs):
            if stage == 1:
                return
            t_ = nc.tensor
            pe.wait_ge(s["b_weights"], 16 * 6)
            with pe.Fori(0, NWIN // 2) as i:
                for u in range(2):
                    w = 2 * i + u
                    G, ends = regs(w, (4, 5))
                    pe.wait_ge(s["b_s_ready"], w + 1)
                    back(w, u, D, (s["rows_ready"], FWIN + w + 1), s["b_agg_done"], s["b_acc_done"],
                         lambda k: ring[:, ds((w % RING) * W + k, 1), 0:D].rearrange("p a b -> p (a b)"))
                    with pe.If(ends > 0):
                        finish_b_pe(pe, G, GT_)
                        hold(pe, "pe_tick")
            finish_b_pe(pe, NG, NT - NG * GT_)
            for r in range(8):
                pe.wait_ge(s["cnt_in"], r + 1)
                t_.matmul(banks[0][:, 0:15], ones[:, :], cnt, start=True, stop=True).then_inc(s["cnt_ps"], 1)
            pe.wait_ge(s["tie_in"], 1)
            t_.matmul(banks[0][:, 0:NT + 1], ones[:, :], tie, start=True, stop=True)
            t_.matmul(banks[1][:, 0:NT], tri, tie[:, 1:NT + 1], start=True, stop=True).then_inc(s["tie_ps"], 1)

        @block.vector
        def _(dve):
            vector_program(dve)

        @block.gpsimd
        def _(pool):
            gpsimd_program(pool)

        @block.sync
        def _(sp):
            sync_program(sp)

        @block.scalar
        def _(act):
            scalar_program(act)

        @block.tensor
        def _(pe):
            tensor_program(pe)



STAGE = 2


def kernel(**inputs):
    import numpy as np
    import concourse.bacc as bacc
    from concourse.bass_utils import run_bass_kernel_spmd as run

    g = {k: np.ascontiguousarray(v) for k, v in inputs.items()}

    def chunks(w):
        return np.ascontiguousarray(w.reshape(-1, P, w.shape[-1]).transpose(1, 0, 2).reshape(P, -1))

    def cols(b):
        return np.ascontiguousarray(b.reshape(-1, P).T)
    edges = np.zeros((EROWS, 2 * P), np.int32)
    edges[:, P:] = NOWHERE
    for side, name in enumerate(("src", "dst")):
        flat = np.full(EROWS * P, NOWHERE if side else 0, np.int32)
        flat[:E] = g[name]
        edges[:, side * P:(side + 1) * P] = flat.reshape(EROWS, P)
    ew = lambda w: np.ascontiguousarray(w.reshape(NX, KD, P, D).transpose(2, 0, 1, 3).reshape(P, -1))
    arrays = {
        "x": g["x"], "edges": edges, "last": np.ascontiguousarray(edges[:, -1].reshape(112, 7)),
        "w0": chunks(g["L0_gnn_W"]),
        "attn": np.concatenate([cols(g["L0_gnn_attn_l"]), cols(g["L0_gnn_attn_r"])], axis=1),
        "bias0": g["L0_gnn_bias"].reshape(1, D),
        "ew0": ew(g["L0_ffn_expert_w1"]), "ew1": ew(g["L0_ffn_expert_w2"]), "ew2": ew(g["L0_ffn_expert_w3"]),
        "eb": np.concatenate([cols(g["L0_ffn_expert_b1"]), cols(g["L0_ffn_expert_b2"])], axis=1),
        "eb3": g["L0_ffn_expert_b3"],
        "rw1": chunks(g["L0_ffn_router_w1"]), "rb1": cols(g["L0_ffn_router_b1"]),
        "rw2": g["L0_ffn_router_w2"], "rb2": g["L0_ffn_router_b2"].reshape(1, NX),
        "w1g": chunks(g["L1_gnn_W"]),
        "wr": cols(g["L1_ffn_wr"].reshape(-1)), "br": g["L1_ffn_br"].reshape(1, 1),
        "fw1": chunks(g["L1_ffn_w1"]), "fb1": cols(g["L1_ffn_b1"]),
        "fw2": chunks(g["L1_ffn_w2"]), "fb2": g["L1_ffn_b2"].reshape(1, D),
    }
    nc = bacc.Bacc("TRN2", target_bir_lowering=False, num_devices=1)
    A = {n: nc.dram_tensor(f"in_{n}", a.shape, mybir.dt.from_np(a.dtype), kind="ExternalInput").ap()
         for n, a in arrays.items()}
    out = nc.dram_tensor("out_0", (N, D), mybir.dt.float32, kind="ExternalOutput").ap()
    gnn_kernel(nc, A, out, STAGE)
    r = run(nc, [{f"in_{n}": a for n, a in arrays.items()}], core_ids=[0])
    return r.results[0]["out_0"]
```
